# Optimizing a Trainium2 kernel written in Bass

```python
import numpy as np
import jax
import jax.numpy as jnp

def _softmax(x, axis=-1):
    return jax.nn.softmax(x, axis=axis)

def _gelu(x):
    return jax.nn.gelu(x, approximate=True)

def _silu(x):
    return jax.nn.silu(x)

def _sigmoid(x):
    return jax.nn.sigmoid(x)

def _layernorm(x, axis=-1, eps=1e-05):
    m = jnp.mean(x, axis=axis, keepdims=True)
    v = jnp.var(x, axis=axis, keepdims=True)
    return (x - m) / jnp.sqrt(v + eps)

def _scatter_add(tgt, idx, src, axis=0):
    return tgt.at[idx].add(src)

def _segment_sum(src, seg, n):
    return jax.ops.segment_sum(src, seg, n)
kernel_name = 'mk_decoder_preln_d1_seqx_r2_9903e0'

def setup_inputs(seed: int=0):
    np.random.seed(seed)
    _w = jnp.asarray

    def _rec_inputs():
        import jax
        import jax.numpy as jnp
        _rk = jax.random.key(seed)
        x = 0.0002417 + 0.9998 * jax.random.normal(jax.random.fold_in(_rk, 1), (16, 512, 512), jnp.float32)
        _lenS = 512 - jax.random.randint(jax.random.fold_in(_rk, 7), (16,), 0, max(1, 512 // 4) + 1, jnp.int32)
        _lenS2 = 120 - jax.random.randint(jax.random.fold_in(_rk, 8), (16,), 0, max(1, 120 // 4) + 1, jnp.int32)
        _ctx_1024P = jax.random.normal(jax.random.fold_in(_rk, 11), (16, 16, 512), jnp.float32)
        _ctx_1024c = jax.random.dirichlet(jax.random.fold_in(_rk, 511), 0.3 * jnp.ones((16,), jnp.float32), (16, 120))
        _ctx_1024t = jnp.einsum('bsk,bkd->bsd', _ctx_1024c, _ctx_1024P)
        _ctx_1024t = _ctx_1024t * jax.lax.rsqrt(jnp.mean(jnp.square(_ctx_1024t)) + 1e-12) * 0.953939
        ctx_1024 = 7.22013e-05 + 1.00017 * (_ctx_1024t + 0.3 * jax.random.normal(jax.random.fold_in(_rk, 611), (16, 120, 512), jnp.float32))
        return (x, ctx_1024)
    x, ctx_1024 = _rec_inputs()

    def _L0_attn_setup():
        import jax, jax.numpy as jnp
        import numpy as np
        D_MODEL = 512
        NUM_HEADS = 16
        MAX_LEN = 1024
        BATCH = 2
        SEQ_LEN = 1024
        key = jax.random.key(seed)
        ks = jax.random.split(key, 6)
        s = 0.02
        return {'x': jax.random.normal(ks[0], (BATCH, SEQ_LEN, D_MODEL), dtype=jnp.float32), 'Wq': jax.random.normal(ks[1], (D_MODEL, D_MODEL), dtype=jnp.float32) * s, 'bq': jnp.zeros((D_MODEL,), dtype=jnp.float32), 'Wk': jax.random.normal(ks[2], (D_MODEL, D_MODEL), dtype=jnp.float32) * s, 'bk': jnp.zeros((D_MODEL,), dtype=jnp.float32), 'Wv': jax.random.normal(ks[3], (D_MODEL, D_MODEL), dtype=jnp.float32) * s, 'bv': jnp.zeros((D_MODEL,), dtype=jnp.float32), 'rel_emb': jax.random.normal(ks[4], (NUM_HEADS, 2 * MAX_LEN - 1), dtype=jnp.float32)}
    _L0_attn_all = _L0_attn_setup()
    _L0_attn_in = {k: v for k, v in _L0_attn_all.items() if k in ('Wq', 'bq', 'Wk', 'bk', 'Wv', 'bv', 'rel_emb')}
    del _L0_attn_all

    def _L0_xattn_setup():
        import jax, jax.numpy as jnp
        import numpy as np
        EMBED = 512
        HEADS = 16
        HEAD_DIM = EMBED // HEADS
        EXP_DIM = 2 * HEAD_DIM

        def _feature_map(x, fm_w, fm_b):
            z = jnp.einsum('nshd,ed->nshe', x, fm_w) + fm_b
            return jnp.concatenate([jnp.exp(z), jnp.exp(-z)], axis=-1)
        key = jax.random.key(seed)
        ks = jax.random.split(key, 7)
        N, S = (4, 1024)
        values = jax.random.normal(ks[0], (N, S, EMBED), dtype=jnp.float32)
        keys_ = jax.random.normal(ks[1], (N, S, EMBED), dtype=jnp.float32)
        query = jax.random.normal(ks[2], (N, S, EMBED), dtype=jnp.float32)
        fm_w = jnp.eye(HEAD_DIM, dtype=jnp.float32) + 0.02 * jax.random.normal(ks[3], (HEAD_DIM, HEAD_DIM), dtype=jnp.float32)
        fm_b = 0.02 * jax.random.normal(ks[4], (HEAD_DIM,), dtype=jnp.float32)
        fc_w = jax.random.normal(ks[5], (EMBED, HEADS * EXP_DIM), dtype=jnp.float32) * (1.0 / np.sqrt(HEADS * EXP_DIM))
        fc_b = jnp.zeros((EMBED,), dtype=jnp.float32)
        return {'values': values, 'keys': keys_, 'query': query, 'fm_w': fm_w, 'fm_b': fm_b, 'fc_w': fc_w, 'fc_b': fc_b}
    _L0_xattn_all = _L0_xattn_setup()
    _L0_xattn_in = {k: v for k, v in _L0_xattn_all.items() if k in ('fm_w', 'fm_b', 'fc_w', 'fc_b')}
    del _L0_xattn_all

    def _L0_ffn_setup():
        import jax, jax.numpy as jnp
        import numpy as np
        DM = 512
        NEXPERTS = 32
        EXPERTSETS = 4
        EXPERTSIZE = 32
        BATCH, SEQ = (4, 1024)
        key = jax.random.key(seed)
        k0, k1, k2, k3 = jax.random.split(key, 4)
        scale = 0.02
        x = jax.random.normal(k0, (BATCH, SEQ, DM), jnp.float32)
        controller = jax.random.normal(k1, (DM, NEXPERTS, EXPERTSETS), jnp.float32) * scale
        f1 = jax.random.normal(k2, (DM, NEXPERTS, EXPERTSETS, EXPERTSIZE), jnp.float32) * scale
        bias = jnp.zeros((NEXPERTS, EXPERTSETS, EXPERTSIZE), jnp.float32)
        f2 = jax.random.normal(k3, (NEXPERTS, EXPERTSETS, EXPERTSIZE, DM), jnp.float32) * scale
        return {'x': x, 'controller': controller, 'f1': f1, 'bias': bias, 'f2': f2}
    _L0_ffn_all = _L0_ffn_setup()
    _L0_ffn_in = {k: v for k, v in _L0_ffn_all.items() if k in ('controller', 'f1', 'bias', 'f2')}
    del _L0_ffn_all
    return {'x': x, 'ctx_1024': ctx_1024, 'L0_attn_Wq': _L0_attn_in['Wq'], 'L0_attn_bq': _L0_attn_in['bq'], 'L0_attn_Wk': _L0_attn_in['Wk'], 'L0_attn_bk': _L0_attn_in['bk'], 'L0_attn_Wv': _L0_attn_in['Wv'], 'L0_attn_bv': _L0_attn_in['bv'], 'L0_attn_rel_emb': _L0_attn_in['rel_emb'], 'L0_xattn_fm_w': _L0_xattn_in['fm_w'], 'L0_xattn_fm_b': _L0_xattn_in['fm_b'], 'L0_xattn_fc_w': _L0_xattn_in['fc_w'], 'L0_xattn_fc_b': _L0_xattn_in['fc_b'], 'L0_ffn_controller': _L0_ffn_in['controller'], 'L0_ffn_f1': _L0_ffn_in['f1'], 'L0_ffn_bias': _L0_ffn_in['bias'], 'L0_ffn_f2': _L0_ffn_in['f2']}

def reference(x, ctx_1024, L0_attn_Wq, L0_attn_bq, L0_attn_Wk, L0_attn_bk, L0_attn_Wv, L0_attn_bv, L0_attn_rel_emb, L0_xattn_fm_w, L0_xattn_fm_b, L0_xattn_fc_w, L0_xattn_fc_b, L0_ffn_controller, L0_ffn_f1, L0_ffn_bias, L0_ffn_f2):
    import jax
    import jax.numpy as jnp

    def _L0_attn_ref(x, Wq, bq, Wk, bk, Wv, bv, rel_emb):
        import jax, jax.numpy as jnp
        import numpy as np
        D_MODEL = 512
        NUM_HEADS = 16
        MAX_LEN = 1024
        BATCH = 2
        SEQ_LEN = 1024
        B, L, D = x.shape
        H = rel_emb.shape[0]
        dk = D // H

        def heads(y):
            return y.reshape(B, L, H, dk).transpose(0, 2, 1, 3)
        q = heads(x @ Wq + bq)
        k = heads(x @ Wk + bk)
        v = heads(x @ Wv + bv)
        scores = jnp.einsum('bhid,bhjd->bhij', q, k) / jnp.sqrt(jnp.float32(dk))
        pos = jnp.arange(L)
        rel_idx = pos[:, None] - pos[None, :] + (L - 1)
        bias = rel_emb[:, rel_idx]
        attn = jax.nn.softmax(scores + bias[None], axis=-1)
        out = jnp.einsum('bhij,bhjd->bhid', attn, v)
        return out.transpose(0, 2, 1, 3).reshape(B, L, D)

    def _L0_xattn_ref(values, keys, query, fm_w, fm_b, fc_w, fc_b):
        import jax, jax.numpy as jnp
        import numpy as np
        EMBED = 512
        HEADS = 16
        HEAD_DIM = EMBED // HEADS
        EXP_DIM = 2 * HEAD_DIM

        def _feature_map(x, fm_w, fm_b):
            z = jnp.einsum('nshd,ed->nshe', x, fm_w) + fm_b
            return jnp.concatenate([jnp.exp(z), jnp.exp(-z)], axis=-1)
        N, S, _ = query.shape
        v = values.reshape(N, -1, HEADS, HEAD_DIM)
        k = keys.reshape(N, -1, HEADS, HEAD_DIM)
        q = query.reshape(N, -1, HEADS, HEAD_DIM)
        v, k, q = (_feature_map(x, fm_w, fm_b) for x in (v, k, q))
        scores = jnp.einsum('nqhd,nkhd->nhqk', q, k) / jnp.sqrt(jnp.float32(EMBED))
        attn = jax.nn.softmax(scores, axis=-1)
        out = jnp.einsum('nhql,nlhd->nqhd', attn, v)
        out = out.reshape(N, S, HEADS * EXP_DIM)
        return out @ fc_w.T + fc_b

    def _L0_ffn_ref(x, controller, f1, bias, f2):
        import jax, jax.numpy as jnp
        import numpy as np
        DM = 512
        NEXPERTS = 32
        EXPERTSETS = 4
        EXPERTSIZE = 32
        BATCH, SEQ = (4, 1024)
        B, L, d = x.shape
        t = controller.shape[1]
        g = L // t
        grouped = x.reshape(B, g, t, d)
        logits = jnp.einsum('bgtd,des->bgtes', grouped, controller)
        tie = jnp.linspace(0.0, 1e-06, t, dtype=logits.dtype).reshape(t, 1, 1)
        logits = logits + tie
        perm = (logits == jnp.max(logits, axis=-3, keepdims=True)).astype(x.dtype)
        perm = jax.lax.stop_gradient(perm)
        dispatched = jnp.einsum('bgtd,bgtes->bgesd', grouped, perm)
        inner = jax.nn.relu(jnp.einsum('bgesd,desf->bgesf', dispatched, f1) + bias)
        intermediate = jnp.einsum('bgesf,esfd->bgesd', inner, f2)
        out = jnp.einsum('bgesd,bgtes->bgtd', intermediate, perm)
        return out.reshape(B, L, d)
    x = x + _L0_attn_ref(_layernorm(x, axis=-1), L0_attn_Wq, L0_attn_bq, L0_attn_Wk, L0_attn_bk, L0_attn_Wv, L0_attn_bv, L0_attn_rel_emb)
    x = x + _L0_xattn_ref(ctx_1024, ctx_1024, _layernorm(x, axis=-1), L0_xattn_fm_w, L0_xattn_fm_b, L0_xattn_fc_w, L0_xattn_fc_b)
    x = x + _L0_ffn_ref(_layernorm(x, axis=-1), L0_ffn_controller, L0_ffn_f1, L0_ffn_bias, L0_ffn_f2)
    return x

_drawn_inputs = setup_inputs


def setup_inputs(seed=0):
    import zlib

    import numpy as np

    out = dict(_drawn_inputs(seed))
    spreads = {'L0_attn_bq': (0.0, 0.8),
     'L0_attn_bk': (0.0, 0.8),
     'L0_attn_bv': (0.0, 0.1),
     'L0_xattn_fc_b': (0.0, 0.8),
     'L0_ffn_bias': (0.0, 0.8)}
    factors = {'L0_attn_Wq': 5.833,
     'L0_attn_Wk': 5.864,
     'L0_ffn_controller': 7.997,
     'L0_ffn_f1': 8.0,
     'L0_ffn_f2': 7.801}
    for name, (base, spread) in spreads.items():
        noise = np.random.default_rng([zlib.crc32(name.encode()), seed]).standard_normal(out[name].shape)
        drawn = base * np.exp(spread * noise) if base else spread * noise
        out[name] = jnp.asarray(drawn.astype(out[name].dtype))
    for name, factor in factors.items():
        out[name] = (out[name] * factor).astype(out[name].dtype)
    return out
```

```python
from contextlib import ExitStack

import concourse.bass as bass
from concourse import mybir

F32 = mybir.dt.float32
F32R = mybir.dt.float32r
ALU = mybir.AluOpType
ACT = mybir.ActivationFunctionType
X = mybir.AxisListType.X

P = 128
EPS = 1e-5
LOWEST = -3.0e38
START = 1


def before(rnd, i, ring, total):
    return rnd * len(range(i % ring, total, ring)) + i // ring


def upto(rnd, i, ring, total):
    return before(rnd, i, ring, total) + 1


def inverse_deviation(pool, nc, mv, veps, minus_half, rstd, tiles, rnd, s_mv, s_veps, s_rstd, waits):
    wait(pool, s_mv, START + tiles * (rnd + 1), waits)
    nc.gpsimd.tensor_scalar(veps[:, :], mv[:, :, 1], EPS, None, ALU.add).then_inc(s_veps, 1)
    pool.wait_ge(s_veps, START + rnd + 1)
    nc.gpsimd.tensor_tensor(rstd[:, :], veps[:, :], minus_half[:, :], ALU.pow).then_inc(s_rstd, 1)


def quadrants(tile, a, n=1):
    return tile[32 * a:32 * (a + n)]


def prime(nc, sems):
    for name, s in sems.items():
        if name not in ("consts", "zeroed", "waits", "nfb_r"):
            nc.gpsimd.sem_inc(s, START)
    nc.all_engine_barrier()


def wait(eng, sem, value, waits):
    eng.wait_ge(sem, value)
    eng.sem_inc(waits, 1)


def layer_norm(eng, nc, x, stats, mv, rstd, tiles, rnd, x_loaded, s_stats, s_mv, s_rstd, s_norm, waits):
    eng.wait_ge(x_loaded, START + 16 * rnd + 16)
    for t in range(tiles):
        nc.vector.bn_stats(stats[:, t, :], x[:, t, :]).then_inc(s_stats, 1)
    wait(eng, s_stats, START + tiles * (rnd + 1), waits)
    for t in range(tiles):
        nc.vector.bn_aggr(mv[:, t, :], stats[:, t, :]).then_inc(s_mv, 1)
    eng.wait_ge(s_rstd, START + rnd + 1)
    for t in range(tiles):
        nc.vector.tensor_scalar(x[:, t, :], x[:, t, :], mv[:, t, 0:1], rstd[:, t:t + 1],
                                ALU.subtract, ALU.mult).then_inc(s_norm, 1)


def self_attention(nc, x_in, x_out, w, ident_in):
    B, L, D = x_in.shape
    H, U = w["skewed"].shape[1:]
    DK = D // H
    T = L // P
    C = D // P
    G = P // DK
    SCALE = float(DK) ** -0.5
    MISC = ["xT"] * C + ["q0", "k0"] + ["v"] * T + ["q1", "k1", "q2", "k2", "o0", "q3", "k3", "o1", "o2", "o3"]
    FIRST_V = MISC.index("v")
    STACK = ((0, 2), (1, 1), (0, 3), (1, 2))
    PER_STACK = 16 * G * len(STACK)
    NM, NS = len(MISC), H * T

    with ExitStack() as ctx:
        sb = lambda name, shape, dt=F32: ctx.enter_context(nc.sbuf_tensor("sa_" + name, shape, dt))
        ps = lambda name: ctx.enter_context(nc.psum_tensor("sa_" + name, [P, L], F32))
        sems = {}

        def sem(name):
            sems[name] = ctx.enter_context(nc.semaphore("sa_" + name))
            return sems[name]

        ident = sb("ident", [P, P])
        wq, wk, wv = (sb(n, [P, C, D]) for n in ("wq", "wk", "wv"))
        bq, bk = sb("bq", [P, C]), sb("bk", [P, C])
        bv = sb("bv", [P, D])
        bias = sb("bias", [P, H, U])
        xn = sb("xn", [P, T, D])
        stats, mv, rstd = sb("stats", [P, T, 6]), sb("mv", [P, T, 2]), sb("rstd", [P, T])
        veps, minus_half = sb("veps", [P, T]), sb("minus_half", [P, T])
        xnT = sb("xnT", [P, C, L])
        res = sb("res", [P, T, D])
        v = sb("v", [P, T, D])
        split = sb("split", [P, 2, 2, L], F32R)
        parts = split[:].rearrange("p w r n -> p (w r) n")
        stack = sb("stack", [P, 2, 2, G, L], F32R)
        top, ntop = sb("top", [P, 2, T]), sb("ntop", [P, 2, T])
        prob = sb("prob", [P, 2, T, L])
        total, rtotal = sb("total", [P, T, H]), sb("rtotal", [P, T, H])
        probT = sb("probT", [P, G, T, L])
        oT = sb("oT", [P, L])
        o = sb("o", [P, T, P])

        ps_s = [ps(f"ps_s{i}") for i in range(3)]
        ps_t = [ps(f"ps_t{i}") for i in range(2)]
        ps_o = ps("ps_o")
        ps_m = [ps(f"ps_m{i}") for i in range(2)]

        consts = sem("consts")
        zeroed = sem("zeroed")
        s_veps = sem("s_veps")
        x_loaded, res_loaded, stored = sem("x_loaded"), sem("res_loaded"), sem("stored")
        s_stats, s_mv, s_rstd, normed = sem("stats_s"), sem("mv_s"), sem("rstd_s"), sem("normed")
        m_full, m_free = [sem(f"m_full{i}") for i in range(2)], [sem(f"m_free{i}") for i in range(2)]
        s_full, s_free = [sem(f"s_full{i}") for i in range(3)], [sem(f"s_free{i}") for i in range(3)]
        t_full, t_free = [sem(f"t_full{i}") for i in range(2)], [sem(f"t_free{i}") for i in range(2)]
        o_full, o_ready = sem("o_full"), sem("o_ready")
        high_ready, stacked = sem("high_ready"), sem("stacked")
        ntop_ready, exp_done, rtotal_ready = sem("ntop_ready"), sem("exp_done"), sem("rtotal_ready")
        res_added = sem("res_added")

        x_tiles = x_in.rearrange("b (t p) d -> b p t d", p=P)
        out_tiles = x_out.rearrange("b (t p) d -> b p t d", p=P)
        nconst = 8
        waits = sem("waits")
        prime(nc, sems)
        block = ctx.enter_context(nc.Block())

        @block.sync
        def _(sp):
            sp.dma_start(xn[:], x_tiles[0]).then_inc(x_loaded, 16)
            sp.dma_start(ident[:], ident_in).then_inc(consts, 16)
            for tile, name in ((wq, "wq"), (wk, "wk"), (wv, "wv")):
                sp.dma_start(tile[:], w[name].rearrange("(c p) n -> p c n", p=P)).then_inc(consts, 16)
            sp.dma_start(bq[:], w["bq"]).then_inc(consts, 16)
            sp.dma_start(bk[:], w["bk"]).then_inc(consts, 16)
            sp.dma_start(bv[:], w["bv"].partition_broadcast(P)).then_inc(consts, 16)
            sp.dma_start(bias[:], w["skewed"]).then_inc(consts, 16)

            def one(b, last):
                wait(sp, stored, START + 16 * b, waits)
                sp.dma_start(res[:], x_tiles[b]).then_inc(res_loaded, 16)
                if not last:
                    for i in (C - 2, C - 1):
                        wait(sp, m_full[i % 2], START + upto(b, i, 2, NM), waits)
                    sp.dma_start(xn[:], x_tiles[b + 1]).then_inc(x_loaded, 16)
                for c in range(C):
                    for kind in "qk":
                        i = MISC.index(f"{kind}{c}")
                        wait(sp, m_free[i % 2], START + upto(b, i, 2, NM), waits)
                    for to, (first, step) in enumerate(STACK):
                        for a in range(G):
                            sp.dma_start(quadrants(stack, to)[:, c % 2, :, a, :].bitcast(F32),
                                         quadrants(parts, a)[:, first:first + step + 1:step, :].bitcast(F32)
                                         ).then_inc(stacked, 16)
                wait(sp, res_added, START + C * b + C, waits)
                sp.dma_start(out_tiles[b], res[:]).then_inc(stored, 16)

            with sp.Fori(0, B - 1) as b:
                one(b, False)
            one(B - 1, True)
            sp.wait_ge(stored, START + 16 * B)

        @block.gpsimd
        def _(pool):
            nc.gpsimd.memset(minus_half[:], -0.5).then_inc(zeroed, 1)
            pool.wait_ge(zeroed, 1)
            def deviation(b):
                inverse_deviation(pool, nc, mv, veps, minus_half, rstd, T, b, s_mv, s_veps, s_rstd, waits)

            def one(b, last):
                pool.wait_ge(res_loaded, START + 16 * b + 16)
                for c in range(C):
                    i = MISC.index(f"o{c}")
                    if c == C - 2 and not last:
                        deviation(b + 1)
                    pool.wait_ge(m_free[i % 2], START + upto(b, i, 2, NM))
                    part = res[:, :, c * P:(c + 1) * P]
                    nc.gpsimd.tensor_tensor(part, part, o[:], ALU.add).then_inc(res_added, 1)

            deviation(0)
            with pool.Fori(0, B - 1) as b:
                one(b, False)
            one(B - 1, True)

        @block.tensor
        def _(pe):
            def misc(b, i):
                pe.wait_ge(m_free[i % 2], START + before(b, i, 2, NM))
                return ps_m[i % 2]

            def project(b, c, kind, wt):
                i = MISC.index(f"{kind}{c}")
                bank = misc(b, i)
                for k in range(C):
                    mm = nc.tensor.matmul(bank[:], wt[:, k, c * P:(c + 1) * P], xnT[:, k, :],
                                          start=(k == 0), stop=(k == C - 1))
                mm.then_inc(m_full[i % 2], 1)

            def scores(b, h):
                c, a = divmod(h, G)
                if a == 0:
                    pe.wait_ge(stacked, START + PER_STACK * (C * b + c + 1))
                for t in range(T):
                    n = h * T + t
                    pe.wait_ge(s_free[n % 3], START + before(b, n, 3, NS))
                    nc.tensor.matmul(ps_s[n % 3][:], stack[:, c % 2, 0, a, t * P:(t + 1) * P], stack[:, c % 2, 1, a, :],
                                     start=True, stop=True).then_inc(s_full[n % 3], 1)

            def transpose_probs(b, h):
                pe.wait_ge(exp_done, START + NS * b + T * (h + 1))
                for j in range(T):
                    n = h * T + j
                    pe.wait_ge(t_free[n % 2], START + before(b, n, 2, NS))
                    for t in range(T):
                        tr = nc.tensor.transpose(ps_t[n % 2][:, t * P:(t + 1) * P],
                                                 prob[:, h % 2, t, j * P:(j + 1) * P], ident[:])
                    tr.then_inc(t_full[n % 2], 1)

            def weigh_values(b, c):
                last = (c + 1) * G * T
                for n in (last - 2, last - 1):
                    pe.wait_ge(t_free[n % 2], START + upto(b, n, 2, NS))
                pe.wait_ge(o_ready, START + C * b + c)
                for j in range(T):
                    for a in range(G):
                        f = (c * G + a) * DK
                        mm = nc.tensor.matmul(ps_o[a * DK:(a + 1) * DK, :], v[:, j, f:f + DK],
                                              probT[:, a, j, :], start=(j == 0), stop=(j == T - 1))
                mm.then_inc(o_full, 1)

            def turn_output(b, c):
                i = MISC.index(f"o{c}")
                pe.wait_ge(o_ready, START + C * b + c + 1)
                bank = misc(b, i)
                for t in range(T):
                    tr = nc.tensor.transpose(bank[:, t * P:(t + 1) * P], oT[:, t * P:(t + 1) * P], ident[:])
                tr.then_inc(m_full[i % 2], 1)

            pe.wait_ge(consts, 16 * nconst)
            with pe.Fori(0, B) as b:
                pe.wait_ge(normed, START + T * b + T)
                for k in range(C):
                    bank = misc(b, k)
                    for t in range(T):
                        tr = nc.tensor.transpose(bank[:, t * P:(t + 1) * P], xn[:, t, k * P:(k + 1) * P], ident[:])
                    tr.then_inc(m_full[k % 2], 1)
                for i in (C - 2, C - 1):
                    pe.wait_ge(m_free[i % 2], START + upto(b, i, 2, NM))
                project(b, 0, "q", wq)
                project(b, 0, "k", wk)
                for t in range(T):
                    i = FIRST_V + t
                    bank = misc(b, i)
                    for k in range(C):
                        mm = nc.tensor.matmul(bank[:], xnT[:, k, t * P:(t + 1) * P], wv[:, k, :],
                                              start=(k == 0), stop=(k == C - 1))
                    mm.then_inc(m_full[i % 2], 1)
                scores(b, 0)
                for h in range(H):
                    if h + 1 < H:
                        scores(b, h + 1)
                    if h % G == 0 and h:
                        weigh_values(b, h // G - 1)
                    transpose_probs(b, h)
                    if h % G == 0 and h + G < H:
                        project(b, h // G + 1, "q", wq)
                        project(b, h // G + 1, "k", wk)
                    if h % G == 1 and h > G:
                        turn_output(b, h // G - 1)
                weigh_values(b, C - 1)
                turn_output(b, C - 1)

        @block.vector
        def _(dve):
            def low_part(b, kind, c):
                which, offset = (0, bq) if kind == "q" else (1, bk)
                i = MISC.index(f"{kind}{c}")
                dve.wait_ge(high_ready, START + 2 * (C * b + c) + which + 1)
                nc.vector.scalar_tensor_tensor(split[:, which, 1], ps_m[i % 2][:], offset[:, c:c + 1],
                                               split[:, which, 0].bitcast(F32), ALU.add, ALU.subtract
                                               ).then_inc(m_free[i % 2], 1)

            def add_bias(b, h):
                if h >= 2:
                    n = (h - 1) * T - 1
                    dve.wait_ge(t_full[n % 2], START + upto(b, n, 2, NS))
                for t in range(T):
                    n = h * T + t
                    wait(dve, s_full[n % 3], START + upto(b, n, 3, NS), waits)
                    off = (T - 1 - t) * P
                    nc.vector.tensor_tensor_reduce(prob[:, h % 2, t, :], ps_s[n % 3][:], bias[:, h, off:off + L],
                                                   1.0, LOWEST, ALU.add, ALU.max,
                                                   top[:, h % 2, t:t + 1]).then_inc(s_free[n % 3], 1)
                for n in range(h * T + 1, h * T + T):
                    dve.wait_ge(s_free[n % 3], START + upto(b, n, 3, NS))
                nc.vector.tensor_scalar(ntop[:, h % 2, :], top[:, h % 2, :], -SCALE, None,
                                        ALU.mult).then_inc(ntop_ready, 1)

            def take_probs(b, h):
                for j in range(0, T, 2):
                    n = h * T + j
                    dve.wait_ge(t_full[n % 2], START + upto(b, n, 2, NS))
                    nc.vector.tensor_copy(probT[:, h % G, j, :], ps_t[n % 2][:]).then_inc(t_free[n % 2], 1)

            def scale_output(b, c):
                i = MISC.index(f"o{c}")
                dve.wait_ge(exp_done, START + NS * b + (c + 1) * G * T)
                nc.vector.reciprocal(rtotal[:, :, c * G:(c + 1) * G],
                                     total[:, :, c * G:(c + 1) * G]).then_inc(rtotal_ready, 1)
                dve.wait_ge(rtotal_ready, START + C * b + c + 1)
                dve.wait_ge(m_full[i % 2], START + upto(b, i, 2, NM))
                dve.wait_ge(res_added, START + C * b + c)
                nc.vector.tensor_tensor(
                    o[:].rearrange("p t (a d) -> p t a d", d=DK),
                    ps_m[i % 2][:].rearrange("p (t a d) -> p t a d", t=T, d=DK),
                    rtotal[:, :, c * G:(c + 1) * G].unsqueeze(3).to_broadcast([P, T, G, DK]),
                    ALU.mult).then_inc(m_free[i % 2], 1)

            def normalise(b):
                layer_norm(dve, nc, xn, stats, mv, rstd, T, b, x_loaded, s_stats, s_mv, s_rstd, normed, waits)

            def one(b, last):
                low_part(b, "q", 0)
                low_part(b, "k", 0)
                for t in range(T):
                    i = FIRST_V + t
                    dve.wait_ge(m_full[i % 2], START + upto(b, i, 2, NM))
                    nc.vector.tensor_tensor(v[:, t, :], ps_m[i % 2][:], bv[:], ALU.add).then_inc(m_free[i % 2], 1)
                add_bias(b, 0)
                for h in range(H):
                    if h + 1 < H:
                        add_bias(b, h + 1)
                    take_probs(b, h)
                    if h % G == 0 and h + G < H:
                        low_part(b, "q", h // G + 1)
                        low_part(b, "k", h // G + 1)
                    if h % G == 1 and h > G:
                        scale_output(b, h // G - 1)
                    if h == H - 6 and not last:
                        normalise(b + 1)
                scale_output(b, C - 1)

            normalise(0)
            dve.wait_ge(consts, 16 * nconst)
            nc.vector.tensor_scalar(bias[:], bias[:], 1.0 / SCALE, None, ALU.mult).then_inc(zeroed, 1)
            dve.wait_ge(zeroed, 2)
            with dve.Fori(0, B - 1) as b:
                one(b, False)
            one(B - 1, True)

        @block.scalar
        def _(act):
            def high_part(b, kind, c):
                which, offset = (0, bq) if kind == "q" else (1, bk)
                i = MISC.index(f"{kind}{c}")
                act.wait_ge(m_full[i % 2], START + upto(b, i, 2, NM))
                if which == 0:
                    act.wait_ge(stacked, START + PER_STACK * (C * b + c))
                nc.scalar.activation(split[:, which, 0], ps_m[i % 2][:], ACT.Identity,
                                     bias=offset[:, c:c + 1]).then_inc(high_ready, 1)

            def exponentiate(b, h):
                act.wait_ge(ntop_ready, START + H * b + h + 1)
                for t in range(T):
                    nc.scalar.activation(prob[:, h % 2, t, :], prob[:, h % 2, t, :], ACT.Exp,
                                         bias=ntop[:, h % 2, t:t + 1], scale=SCALE,
                                         accum_out=total[:, t, h:h + 1]).then_inc(exp_done, 1)

            def take_probs(b, h):
                for j in range(1, T, 2):
                    n = h * T + j
                    act.wait_ge(t_full[n % 2], START + upto(b, n, 2, NS))
                    nc.scalar.copy(probT[:, h % G, j, :], ps_t[n % 2][:]).then_inc(t_free[n % 2], 1)

            def take_output(b, c):
                act.wait_ge(o_full, START + C * b + c + 1)
                nc.scalar.copy(oT[:], ps_o[:]).then_inc(o_ready, 1)

            act.wait_ge(consts, 16 * nconst)
            with act.Fori(0, B) as b:
                for k in range(C):
                    act.wait_ge(m_full[k % 2], START + upto(b, k, 2, NM))
                    nc.scalar.copy(xnT[:, k, :], ps_m[k % 2][:]).then_inc(m_free[k % 2], 1)
                high_part(b, "q", 0)
                high_part(b, "k", 0)
                exponentiate(b, 0)
                for h in range(H):
                    if h + 1 < H:
                        exponentiate(b, h + 1)
                    if h % G == 0 and h:
                        take_output(b, h // G - 1)
                    take_probs(b, h)
                    if h % G == 0 and h + G < H:
                        high_part(b, "q", h // G + 1)
                        high_part(b, "k", h // G + 1)
                take_output(b, C - 1)


def cross_attention(nc, x_in, x_out, context, w, ident_in, quads_in):
    B, L, D = x_in.shape
    S = context.shape[1]
    DK = w["fm"].shape[0]
    H = D // DK
    T, C, G = L // P, D // P, P // DK
    E = 2 * DK
    PAIRS = H // 2
    SCALE = float(D) ** -0.5
    MISC = ["cT", "cz", "cv"] + ["xT"] * C + ["z"] * C + ["fc"] * T
    NM, NS = len(MISC), T * C

    with ExitStack() as ctx:
        sb = lambda name, shape: ctx.enter_context(nc.sbuf_tensor("ca_" + name, shape, F32))
        ps = lambda name: ctx.enter_context(nc.psum_tensor("ca_" + name, [P, L], F32))
        sems = {}

        def sem(name):
            sems[name] = ctx.enter_context(nc.semaphore("ca_" + name))
            return sems[name]

        ident, quads = sb("ident", [P, P]), sb("quads", [P, G])
        fm = sb("fm", [P, P])
        fb, nfb, fb_row = sb("fb", [P, 1]), sb("nfb", [P, 1]), sb("fb_row", [P, D])
        fc, fcb = sb("fc", [P, PAIRS, D]), sb("fcb", [P, D])
        con = sb("con", [S, D])
        conT = sb("conT", [P, C, S])
        kexp = sb("kexp", [P, 2, C, S])
        kfeat = sb("kfeat", [P, 2, C, G, S])
        vz = sb("vz", [S, D])
        vfeat = sb("vfeat", [S, H, E])
        xn, res = sb("xn", [P, T, D]), sb("res", [P, T, D])
        stats, mv, rstd = sb("stats", [P, T, 6]), sb("mv", [P, T, 2]), sb("rstd", [P, T])
        veps, minus_half = sb("veps", [P, T]), sb("minus_half", [P, T])
        xnT = sb("xnT", [P, C, L])
        qexp = sb("qexp", [P, 2, C, L])
        top = sb("top", [P, NS, G])
        prob = sb("prob", [P, T, H, S])
        total, rtotal = sb("total", [P, T, H]), sb("rtotal", [P, T, H])
        probT = sb("probT", [S, H, L])
        oT = sb("oT", [P, PAIRS, L])

        ps_s = [ps(f"ps_s{i}") for i in range(3)]
        ps_t = [ps(f"ps_t{i}") for i in range(2)]
        ps_o = ps("ps_o")
        ps_m = [ps(f"ps_m{i}") for i in range(2)]

        consts, zeroed = sem("consts"), sem("zeroed")
        x_loaded, con_loaded, res_loaded, stored = (sem(n) for n in ("x_l", "con_l", "res_l", "stored"))
        s_stats, s_mv, s_rstd, s_veps, normed = (sem(n) for n in ("stats_s", "mv_s", "rstd_s", "veps_s", "normed"))
        m_full, m_free = [sem(f"m_full{i}") for i in range(2)], [sem(f"m_free{i}") for i in range(2)]
        s_full, s_free = [sem(f"s_full{i}") for i in range(3)], [sem(f"s_free{i}") for i in range(3)]
        t_full, t_free = [sem(f"t_full{i}") for i in range(2)], [sem(f"t_free{i}") for i in range(2)]
        o_full, o_ready = sem("o_full"), sem("o_ready")
        nfb_ready, kexp_ready, kfeat_ready, vz_ready, vfeat_ready = (
            sem(n) for n in ("nfb_r", "kexp_r", "kfeat_r", "vz_r", "vfeat_r"))
        top_ready, exp_done, total_ready, rtotal_ready = (sem(n) for n in ("top_r", "exp_d", "total_r", "rtotal_r"))
        prob_ready, res_biased = sem("prob_r"), sem("res_b")

        x_tiles = x_in.rearrange("b (t p) d -> b p t d", p=P)
        out_tiles = x_out.rearrange("b (t p) d -> b p t d", p=P)
        nconst = 6 + G
        waits = sem("waits")
        prime(nc, sems)
        block = ctx.enter_context(nc.Block())

        @block.sync
        def _(sp):
            sp.dma_start(con[:], context[0]).then_inc(con_loaded, 16)
            sp.dma_start(xn[:], x_tiles[0]).then_inc(x_loaded, 16)
            sp.wait_ge(zeroed, 2)
            for a in range(G):
                sp.dma_start(quadrants(fm, a)[:, a * DK:(a + 1) * DK], w["fm"]).then_inc(consts, 16)
            for tile, src in ((ident[:], ident_in), (quads[:], quads_in), (fb[:], w["fb"]),
                              (fb_row[:], w["fb_row"].partition_broadcast(P)),
                              (fc[:], w["fc"].rearrange("(c p) n -> p c n", p=P)),
                              (fcb[:], w["fcb"].partition_broadcast(P))):
                sp.dma_start(tile, src).then_inc(consts, 16)

            def one(b, last):
                wait(sp, stored, START + 16 * b, waits)
                sp.dma_start(res[:], x_tiles[b]).then_inc(res_loaded, 16)
                if not last:
                    wait(sp, m_full[0], START + upto(b, 0, 2, NM), waits)
                    sp.dma_start(con[:], context[b + 1]).then_inc(con_loaded, 16)
                    for i in (C + 1, C + 2):
                        wait(sp, m_full[i % 2], START + upto(b, i, 2, NM), waits)
                    sp.dma_start(xn[:], x_tiles[b + 1]).then_inc(x_loaded, 16)
                for i in (NM - 2, NM - 1):
                    wait(sp, m_free[i % 2], START + upto(b, i, 2, NM), waits)
                sp.dma_start(out_tiles[b], res[:]).then_inc(stored, 16)

            with sp.Fori(0, B - 1) as b:
                one(b, False)
            one(B - 1, True)
            sp.wait_ge(stored, START + 16 * B)

        @block.gpsimd
        def _(pool):
            nc.gpsimd.memset(fm[:], 0.0).then_inc(zeroed, 1)
            nc.gpsimd.memset(minus_half[:], -0.5).then_inc(zeroed, 1)
            pool.wait_ge(zeroed, 2)
            pool.wait_ge(consts, 16 * nconst)
            with pool.Fori(0, B) as b:
                inverse_deviation(pool, nc, mv, veps, minus_half, rstd, T, b, s_mv, s_veps, s_rstd, waits)
                pool.wait_ge(kexp_ready, START + 2 * b + 2)
                for g in range(2):
                    for a in range(G):
                        nc.gpsimd.tensor_tensor(kfeat[:, g, :, a, :], kexp[:, g],
                                                quads[:, a:a + 1].unsqueeze(2).to_broadcast([P, C, S]),
                                                ALU.mult).then_inc(kfeat_ready, 1)
                pool.wait_ge(res_loaded, START + 16 * b + 16)
                nc.gpsimd.tensor_tensor(res[:], res[:], fcb[:].unsqueeze(1).to_broadcast([P, T, D]),
                                        ALU.add).then_inc(res_biased, 1)
                for t in range(T):
                    pool.wait_ge(rtotal_ready, START + T * b + t + 1)
                    nc.gpsimd.tensor_tensor(prob[:, t], prob[:, t],
                                            rtotal[:, t, :].unsqueeze(2).to_broadcast([P, H, S]),
                                            ALU.mult).then_inc(prob_ready, 1)

        @block.tensor
        def _(pe):
            def misc(b, i):
                pe.wait_ge(m_free[i % 2], START + before(b, i, 2, NM))
                return ps_m[i % 2]

            def taken(b, i):
                pe.wait_ge(m_free[i % 2], START + upto(b, i, 2, NM))

            pe.wait_ge(consts, 16 * nconst)
            with pe.Fori(0, B) as b:
                pe.wait_ge(con_loaded, START + 16 * b + 16)
                bank = misc(b, 0)
                for c in range(C):
                    tr = nc.tensor.transpose(bank[:, c * S:(c + 1) * S], con[:, c * P:(c + 1) * P], ident[0:S, 0:S])
                tr.then_inc(m_full[0], 1)
                taken(b, 0)
                bank = misc(b, 1)
                for c in range(C):
                    mm = nc.tensor.matmul(bank[:, c * S:(c + 1) * S], fm[:], conT[:, c, :], start=True, stop=True)
                mm.then_inc(m_full[1], 1)
                bank = misc(b, 2)
                for c in range(C):
                    mm = nc.tensor.matmul(bank[0:S, c * P:(c + 1) * P], conT[:, c, :], fm[:], start=True, stop=True)
                mm.then_inc(m_full[0], 1)
                pe.wait_ge(normed, START + T * b + T)
                for k in range(C):
                    i = 3 + k
                    bank = misc(b, i)
                    for t in range(T):
                        tr = nc.tensor.transpose(bank[:, t * P:(t + 1) * P], xn[:, t, k * P:(k + 1) * P], ident[:])
                    tr.then_inc(m_full[i % 2], 1)
                for c in range(C):
                    i = 3 + C + c
                    taken(b, 3 + c)
                    bank = misc(b, i)
                    nc.tensor.matmul(bank[:], fm[:], xnT[:, c, :], start=True, stop=True).then_inc(m_full[i % 2], 1)
                for c in range(C - 2, C):
                    taken(b, 3 + C + c)
                pe.wait_ge(kfeat_ready, START + 2 * G * (b + 1))
                for n in range(NS):
                    t, c = divmod(n, C)
                    pe.wait_ge(s_free[n % 3], START + before(b, n, 3, NS))
                    for g in range(2):
                        mm = nc.tensor.matmul(ps_s[n % 3][:, 0:G * S], qexp[:, g, c, t * P:(t + 1) * P],
                                              kfeat[:, g, c].rearrange("p a s -> p (a s)"),
                                              start=(g == 0), stop=(g == 1))
                    mm.then_inc(s_full[n % 3], 1)
                pe.wait_ge(vfeat_ready, START + 2 * b + 2)

                def weigh_values(r):
                    for h in (2 * r, 2 * r + 1):
                        pe.wait_ge(t_free[h % 2], START + upto(b, h, 2, H))
                    pe.wait_ge(o_ready, START + PAIRS * b + r)
                    for a in range(2):
                        mm = nc.tensor.matmul(ps_o[a * E:(a + 1) * E, :], vfeat[:, 2 * r + a, :],
                                              probT[:, 2 * r + a, :], start=True, stop=True)
                    mm.then_inc(o_full, 1)

                pe.wait_ge(prob_ready, START + T * b + T)
                for h in range(H):
                    pe.wait_ge(t_free[h % 2], START + before(b, h, 2, H))
                    for t in range(T):
                        tr = nc.tensor.transpose(ps_t[h % 2][0:S, t * P:(t + 1) * P], prob[:, t, h, :], ident[:])
                    tr.then_inc(t_full[h % 2], 1)
                    if h % 2 == 1 and h > 2:
                        weigh_values(h // 2 - 1)
                weigh_values(PAIRS - 1)
                pe.wait_ge(o_ready, START + PAIRS * (b + 1))
                for t in range(T):
                    i = 3 + 2 * C + t
                    bank = misc(b, i)
                    for r in range(PAIRS):
                        mm = nc.tensor.matmul(bank[:], oT[:, r, t * P:(t + 1) * P], fc[:, r, :],
                                              start=(r == 0), stop=(r == PAIRS - 1))
                    mm.then_inc(m_full[i % 2], 1)

        @block.vector
        def _(dve):
            def filled(b, i):
                dve.wait_ge(m_full[i % 2], START + upto(b, i, 2, NM))
                return ps_m[i % 2]

            def sums(dve, b, t):
                dve.wait_ge(exp_done, START + T * b + t + 1)
                nc.vector.tensor_reduce(total[:, t, :], prob[:, t], X, ALU.add).then_inc(total_ready, 1)
                dve.wait_ge(total_ready, START + T * b + t + 1)
                nc.vector.reciprocal(rtotal[:, t, :], total[:, t, :]).then_inc(rtotal_ready, 1)

            dve.wait_ge(consts, 16 * nconst)
            nc.vector.tensor_scalar(nfb[:], fb[:], -1.0, None, ALU.mult).then_inc(nfb_ready, 1)
            with dve.Fori(0, B) as b:
                bank = filled(b, 2)
                nc.vector.tensor_tensor(vz[:], bank[0:S, :], fb_row[0:S, :], ALU.add).then_inc(m_free[0], 1)
                layer_norm(dve, nc, xn, stats, mv, rstd, T, b, x_loaded, s_stats, s_mv, s_rstd, normed, waits)
                for n in range(NS):
                    t, c = divmod(n, C)
                    dve.wait_ge(s_full[n % 3], START + upto(b, n, 3, NS))
                    bank = ps_s[n % 3][:, 0:G * S].rearrange("p (a s) -> p a s", s=S)
                    nc.vector.tensor_reduce(top[:, n, :], bank, X, ALU.max).then_inc(top_ready, 1)
                    dve.wait_ge(top_ready, START + NS * b + n + 1)
                    nc.vector.tensor_tensor(prob[:, t, c * G:(c + 1) * G, :], bank,
                                            top[:, n, :].unsqueeze(2).to_broadcast([P, G, S]),
                                            ALU.subtract).then_inc(s_free[n % 3], 1)
                    if c == C - 1 and t > 0:
                        sums(dve, b, t - 1)
                sums(dve, b, T - 1)
                for h in range(0, H, 2):
                    dve.wait_ge(t_full[0], START + upto(b, h, 2, H))
                    nc.vector.tensor_copy(probT[:, h, :], ps_t[0][0:S, :]).then_inc(t_free[0], 1)
                dve.wait_ge(res_biased, START + b + 1)
                for t in range(T):
                    i = 3 + 2 * C + t
                    bank = filled(b, i)
                    nc.vector.tensor_tensor(res[:, t, :], res[:, t, :], bank[:], ALU.add).then_inc(m_free[i % 2], 1)

        @block.scalar
        def _(act):
            def filled(b, i):
                act.wait_ge(m_full[i % 2], START + upto(b, i, 2, NM))
                return ps_m[i % 2]

            act.wait_ge(consts, 16 * nconst)
            act.wait_ge(nfb_ready, 1)
            with act.Fori(0, B) as b:
                bank = filled(b, 0)
                nc.scalar.copy(conT[:].rearrange("p c s -> p (c s)"), bank[:, 0:C * S]).then_inc(m_free[0], 1)
                bank = filled(b, 1)
                for g, (sign, offset) in enumerate(((1.0, fb), (-1.0, nfb))):
                    op = nc.scalar.activation(kexp[:, g].rearrange("p c s -> p (c s)"), bank[:, 0:C * S], ACT.Exp,
                                              bias=offset[:], scale=sign).then_inc(kexp_ready, 1)
                act.wait_ge(kexp_ready, START + 2 * b + 2)
                act.sem_inc(m_free[1], 1)
                act.wait_ge(m_free[0], START + upto(b, 2, 2, NM))
                for g in range(2):
                    nc.scalar.activation(vfeat[:, :, g * DK:(g + 1) * DK], vz[:].rearrange("p (h e) -> p h e", e=DK),
                                         ACT.Exp, scale=1.0 - 2.0 * g).then_inc(vfeat_ready, 1)
                for k in range(C):
                    bank = filled(b, 3 + k)
                    nc.scalar.copy(xnT[:, k, :], bank[:]).then_inc(m_free[(3 + k) % 2], 1)
                for c in range(C):
                    i = 3 + C + c
                    bank = filled(b, i)
                    nc.scalar.activation(qexp[:, 0, c, :], bank[:], ACT.Exp, bias=fb[:])
                    nc.scalar.activation(qexp[:, 1, c, :], bank[:], ACT.Exp, bias=nfb[:],
                                         scale=-1.0).then_inc(m_free[i % 2], 1)
                for t in range(T):
                    n = t * C + C - 1
                    for i in range(n - 2, n + 1):
                        act.wait_ge(s_free[i % 3], START + upto(b, i, 3, NS))
                    nc.scalar.activation(prob[:, t], prob[:, t], ACT.Exp, scale=SCALE).then_inc(exp_done, 1)

                def take_output(r):
                    act.wait_ge(o_full, START + PAIRS * b + r + 1)
                    nc.scalar.copy(oT[:, r, :], ps_o[:]).then_inc(o_ready, 1)

                for h in range(1, H, 2):
                    act.wait_ge(t_full[1], START + upto(b, h, 2, H))
                    nc.scalar.copy(probT[:, h, :], ps_t[1][0:S, :]).then_inc(t_free[1], 1)
                    if h > 2:
                        take_output(h // 2 - 1)
                take_output(PAIRS - 1)


def expert_ffn(nc, x_in, x_out, scratch, w, ident_in, quads_in):
    B, L, D = x_in.shape
    R = 4
    ROUNDS = B // R
    T, C, Q = L // P, D // P, 4
    TG = w["tie"].shape[0]
    ES = w["controller"].shape[1]
    F = w["f1"].shape[1] // ES
    GROUPS = R * L // TG
    QUADS = ES // Q
    TILES = R * T
    W = 2
    PER = C + 2
    NM = R * PER
    ND = TILES * C
    NF, NY = QUADS, 2 * QUADS
    NLOAD = QUADS // W

    with ExitStack() as ctx:
        sb = lambda name, shape: ctx.enter_context(nc.sbuf_tensor("ff_" + name, shape, F32))
        ps = lambda name: ctx.enter_context(nc.psum_tensor("ff_" + name, [P, L], F32))
        sems = {}

        def sem(name):
            sems[name] = ctx.enter_context(nc.semaphore("ff_" + name))
            return sems[name]

        ident, quads = sb("ident", [P, P]), sb("quads", [P, Q])
        ctrl, tie, bias1 = sb("ctrl", [P, C, ES]), sb("tie", [P, TG]), sb("bias1", [P, QUADS])
        work = sb("work", [P, 2, T, D])
        xn, xnT = work[:, 0], work[:, 1]
        stats, mv, rstd = sb("stats", [P, T, 6]), sb("mv", [P, T, 2]), sb("rstd", [P, T])
        veps, minus_half = sb("veps", [P, T]), sb("minus_half", [P, T])
        logit, best = sb("logit", [P, L]), sb("best", [P, L // TG])
        pick = sb("pick", [P, R * L])
        picked = sb("picked", [P, 2, Q, ES])
        taken = sb("taken", [P, C, GROUPS, ES])
        f1 = sb("f1", [P, 2, C, W * Q * F])
        f2 = sb("f2", [P, 2, W, D])
        inner = sb("inner", [P, 2, GROUPS])
        inner_q = sb("inner_q", [P, 2, Q, GROUPS])
        y = sb("y", [P, 4, D])
        res = sb("res", [P, 2, D])

        ps_m = [ps(f"ps_m{i}") for i in range(2)]
        ps_d = [ps(f"ps_d{i}") for i in range(3)]
        ps_f = [ps(f"ps_f{i}") for i in range(2)]
        names = "consts zeroed x_l stats_s mv_s rstd_s veps_s normed best_r pick_r picked_r " \
                "f1_l f2_l inner_r innerq_r y_st yrow_l0 yrow_l1 res_l0 res_l1 stored0 stored1".split()
        S = {n: sem(n) for n in names}
        ring = lambda name, n: [sem(f"{name}{i}") for i in range(n)]
        m_full, m_free = ring("m_full", 2), ring("m_free", 2)
        d_full, d_free = ring("d_full", 3), ring("d_free", 3)
        y_full, y_free, y_stored = ring("y_full", 3), ring("y_free", 3), ring("y_stored", 4)
        f_full, f_free = ring("f_full", 2), ring("f_free", 2)
        c_full, c_free = ring("c_full", 2), ring("c_free", 2)
        f1_l, f2_l = ring("f1l", 2), ring("f2l", 2)

        x_tiles = x_in.rearrange("b (t p) d -> b p t d", p=P)
        x_rows = x_in.rearrange("(r s) (t p) d -> r (s t) p d", s=R, p=P)
        out_rows = x_out.rearrange("(r s) (t p) d -> r (s t) p d", s=R, p=P)
        f1_v = w["f1"].rearrange("(c p) n -> p c n", p=P)
        f2_v = w["f2"].rearrange("(q p) n -> p q n", p=P)
        nconst = 5
        waits = sem("waits")
        prime(nc, sems)
        block = ctx.enter_context(nc.Block())

        @block.sync
        def _(sp):
            for tile, src in ((ident[:], ident_in), (quads[:], quads_in), (bias1[:], w["bias1"]),
                              (ctrl[:], w["controller"].rearrange("(c p) n -> p c n", p=P)),
                              (tie[:], w["tie"].partition_broadcast(P))):
                sp.dma_start(tile, src).then_inc(S["consts"], 16)

            with sp.Fori(0, ROUNDS) as r:
                for s in range(R):
                    if s == 0:
                        wait(sp, c_full[(TILES - 1) % 2], START + r * (TILES // 2), waits)
                        sp.dma_start(xn, x_tiles[r * R]).then_inc(S["x_l"], 16)
                    else:
                        for n in range(s * T * C - 3, s * T * C):
                            wait(sp, d_full[n % 3], START + upto(r, n, 3, ND), waits)
                        sp.dma_start(xn, x_tiles[r * R + s]).then_inc(S["x_l"], 16)

                def weights(n):
                    if n < 2:
                        for q in (QUADS - 2, QUADS - 1):
                            wait(sp, f_full[q % 2], START + r * (NF // 2), waits)
                        for i in range(NY - 3, NY):
                            wait(sp, y_full[i % 3], START + r * len(range(i % 3, NY, 3)), waits)
                    else:
                        q = (n - 2) * W + W - 1
                        for i in (q - 1, q):
                            wait(sp, f_full[i % 2], START + upto(r, i, 2, NF), waits)
                        wait(sp, y_full[(2 * q + 1) % 3], START + upto(r, 2 * q + 1, 3, NY), waits)
                    sp.dma_start(f1[:, n % 2], f1_v[:, :, n * W * Q * F:(n + 1) * W * Q * F]).then_inc(f1_l[n % 2], 16)
                    sp.dma_start(f2[:, n % 2], f2_v[:, n * W:(n + 1) * W, :]).then_inc(f2_l[n % 2], 16)

                weights(0)
                weights(1)
                for q in range(QUADS):
                    for j in range(2):
                        n = 2 * q + j
                        wait(sp, y_free[n % 3], START + upto(r, n, 3, NY), waits)
                        for a in range(2):
                            e = Q * q + 2 * j + a
                            sp.dma_start(scratch[r, :, e, :], y[a * GROUPS:(a + 1) * GROUPS, n % 4, :]
                                         ).then_inc(y_stored[n % 4], 16)
                    if q % W == W - 1 and q // W + 2 < NLOAD:
                        weights(q // W + 2)
                for i in range(4):
                    wait(sp, y_stored[i], START + 32 * (NY // 4) * (r + 1), waits)
                for n in range(TILES):
                    if n >= 2:
                        wait(sp, c_full[n % 2], START + before(r, n, 2, TILES), waits)
                        wait(sp, S["stored0" if n % 2 == 0 else "stored1"], START + 16 * before(r, n, 2, TILES), waits)
                    else:
                        wait(sp, S["stored0" if n % 2 == 0 else "stored1"], START + 16 * r * (TILES // 2), waits)
                    sp.dma_start(work[:, n % 2], scratch[r, n * Q:(n + 1) * Q].rearrange("g e d -> e g d")
                                 ).then_inc(S[f"yrow_l{n % 2}"], 16)
                    sp.dma_start(res[:, n % 2], x_rows[r, n]).then_inc(S[f"res_l{n % 2}"], 16)
            for i in range(2):
                sp.wait_ge(S[f"stored{i}"], START + 16 * ROUNDS * (TILES // 2))

        @block.gpsimd
        def _(pool):
            nc.gpsimd.memset(minus_half[:], -0.5).then_inc(S["zeroed"], 1)
            pool.wait_ge(S["zeroed"], 1)
            with pool.Fori(0, ROUNDS) as r:
                for s in range(R):
                    inverse_deviation(pool, nc, mv, veps, minus_half, rstd, T, r * R + s, S["mv_s"], S["veps_s"],
                                      S["rstd_s"], waits)

        @block.tensor
        def _(pe):
            def misc(r, i):
                pe.wait_ge(m_free[i % 2], START + before(r, i, 2, NM))
                return ps_m[i % 2]

            pe.wait_ge(S["consts"], 16 * nconst)
            with pe.Fori(0, ROUNDS) as r:
                for s in range(R):
                    pe.wait_ge(S["normed"], START + T * R * r + T * (s + 1))
                    for k in range(C):
                        i = s * PER + k
                        bank = misc(r, i)
                        for t in range(T):
                            tr = nc.tensor.transpose(bank[:, t * P:(t + 1) * P], xn[:, t, k * P:(k + 1) * P], ident[:])
                        tr.then_inc(m_full[i % 2], 1)
                    for k in (C - 2, C - 1):
                        pe.wait_ge(m_free[(s * PER + k) % 2], START + upto(r, s * PER + k, 2, NM))
                    i = s * PER + C
                    bank = misc(r, i)
                    for k in range(C):
                        mm = nc.tensor.matmul(bank[:], ctrl[:, k, :], xnT[:, k, :], start=(k == 0), stop=(k == C - 1))
                    mm.then_inc(m_full[i % 2], 1)
                    pe.wait_ge(S["pick_r"], START + R * r + s + 1)
                    i = s * PER + C + 1
                    bank = misc(r, i)
                    for t in range(T):
                        at = (s * T + t) * P
                        tr = nc.tensor.transpose(bank[:, t * P:(t + 1) * P], pick[:, at:at + P], ident[:])
                    tr.then_inc(m_full[i % 2], 1)
                    for t in range(T):
                        pe.wait_ge(S["picked_r"], START + TILES * r + s * T + t + 1)
                        for k in range(C):
                            n = (s * T + t) * C + k
                            pe.wait_ge(d_free[n % 3], START + before(r, n, 3, ND))
                            if n < 3:
                                pe.wait_ge(y_free[n], START + r * len(range(n, NY, 3)))
                            nc.tensor.matmul(ps_d[n % 3][:], xn[:, t, k * P:(k + 1) * P],
                                             picked[:, t % 2].rearrange("p g e -> p (g e)"),
                                             start=True, stop=True).then_inc(d_full[n % 3], 1)
                for n in range(ND - 3, ND):
                    pe.wait_ge(d_free[n % 3], START + upto(r, n, 3, ND))

                def inner_layer(q):
                    if q % W == 0:
                        pe.wait_ge(f1_l[q // W % 2], START + 16 * upto(r, q // W, 2, NLOAD))
                    pe.wait_ge(f_free[q % 2], START + before(r, q, 2, NF))
                    if q < 2:
                        pe.wait_ge(c_free[q % 2], START + r * (TILES // 2))
                    for k in range(C):
                        for a in range(Q):
                            f = (q % W * Q + a) * F
                            mm = nc.tensor.matmul(ps_f[q % 2][a * F:(a + 1) * F, 0:GROUPS],
                                                  f1[:, q // W % 2, k, f:f + F], taken[:, k, :, Q * q + a],
                                                  start=(k == 0), stop=(k == C - 1))
                    mm.then_inc(f_full[q % 2], 1)

                def outer_layer(q):
                    if q % W == 0:
                        pe.wait_ge(f2_l[q // W % 2], START + 16 * upto(r, q // W, 2, NLOAD))
                    pe.wait_ge(S["innerq_r"], START + QUADS * r + q + 1)
                    for j in range(2):
                        n = 2 * q + j
                        pe.wait_ge(y_free[n % 3], START + before(r, n, 3, NY))
                        mm = nc.tensor.matmul(ps_d[n % 3][:], inner_q[:, q % 2, 2 * j:2 * j + 2, :].rearrange(
                            "p a g -> p (a g)"), f2[:, q // W % 2, q % W, :], start=True, stop=True)
                        mm.then_inc(y_full[n % 3], 1)

                inner_layer(0)
                for q in range(QUADS):
                    if q + 1 < QUADS:
                        inner_layer(q + 1)
                    outer_layer(q)
                for n in range(TILES):
                    pe.wait_ge(S[f"yrow_l{n % 2}"], START + 16 * upto(r, n, 2, TILES))
                    pe.wait_ge(c_free[n % 2], START + before(r, n, 2, TILES))
                    if n < 2:
                        pe.wait_ge(f_free[n % 2], START + (r + 1) * (NF // 2))
                    for g in range(Q):
                        at = (n * Q + g) * TG
                        mm = nc.tensor.matmul(ps_f[n % 2][g * TG:(g + 1) * TG, :], pick[:, at:at + TG],
                                              work[:, n % 2, g, :], start=True, stop=True)
                    mm.then_inc(c_full[n % 2], 1)

        def take(eng, r, n):
            t, k = divmod(n, C)
            eng.wait_ge(d_full[n % 3], START + upto(r, n, 3, ND))
            dst = taken[:, k, t * Q:(t + 1) * Q, :].rearrange("p g e -> p (g e)")
            copy = nc.vector.tensor_copy if k % 2 == 0 else nc.scalar.copy
            copy(dst, ps_d[n % 3][:]).then_inc(d_free[n % 3], 1)

        @block.vector
        def _(dve):
            dve.wait_ge(S["consts"], 16 * nconst)
            with dve.Fori(0, ROUNDS) as r:
                for s in range(R):
                    layer_norm(dve, nc, xn, stats, mv, rstd, T, r * R + s, S["x_l"], S["stats_s"], S["mv_s"],
                               S["rstd_s"], S["normed"], waits)
                    i = s * PER + C
                    dve.wait_ge(m_full[i % 2], START + upto(r, i, 2, NM))
                    by_group = lambda ap: ap.rearrange("p (g t) -> p g t", t=TG)
                    nc.vector.tensor_tensor(by_group(logit[:]), by_group(ps_m[i % 2][:]),
                                            tie[:].unsqueeze(1).to_broadcast([P, L // TG, TG]),
                                            ALU.add).then_inc(m_free[i % 2], 1)
                    dve.wait_ge(m_free[i % 2], START + upto(r, i, 2, NM))
                    nc.vector.tensor_reduce(best[:], by_group(logit[:]), X, ALU.max).then_inc(S["best_r"], 1)
                    dve.wait_ge(S["best_r"], START + R * r + s + 1)
                    nc.vector.tensor_tensor(by_group(pick[:, s * L:(s + 1) * L]), by_group(logit[:]),
                                            best[:].unsqueeze(2).to_broadcast([P, L // TG, TG]),
                                            ALU.is_equal).then_inc(S["pick_r"], 1)
                    i = s * PER + C + 1
                    dve.wait_ge(m_full[i % 2], START + upto(r, i, 2, NM))
                    for t in range(T):
                        if t >= 2:
                            n = (s * T + t - 1) * C - 1
                            dve.wait_ge(d_full[n % 3], START + upto(r, n, 3, ND))
                        nc.vector.tensor_tensor(picked[:, t % 2],
                                                ps_m[i % 2][:, t * P:(t + 1) * P].unsqueeze(1).to_broadcast([P, Q, ES]),
                                                quads[:].unsqueeze(2).to_broadcast([P, Q, ES]),
                                                ALU.mult).then_inc(S["picked_r"], 1)
                        if t >= 1:
                            take(dve, r, (s * T + t - 1) * C)
                            take(dve, r, (s * T + t - 1) * C + 2)
                    dve.wait_ge(S["picked_r"], START + TILES * r + T * (s + 1))
                    dve.sem_inc(m_free[i % 2], 1)
                    take(dve, r, (s * T + T - 1) * C)
                    take(dve, r, (s * T + T - 1) * C + 2)

                def rows(q):
                    n = 2 * q
                    dve.wait_ge(y_full[n % 3], START + upto(r, n, 3, NY))
                    if n >= 4:
                        dve.wait_ge(y_stored[n % 4], START + 32 * before(r, n, 4, NY))
                    nc.vector.tensor_copy(y[:, n % 4, :], ps_d[n % 3][:]).then_inc(y_free[n % 3], 1)

                for q in range(QUADS):
                    dve.wait_ge(f_full[q % 2], START + upto(r, q, 2, NF))
                    nc.vector.tensor_scalar(inner[:, q % 2, :], ps_f[q % 2][:, 0:GROUPS], bias1[:, q:q + 1], 0.0,
                                            ALU.add, ALU.max).then_inc(f_free[q % 2], 1)
                    dve.wait_ge(f_free[q % 2], START + upto(r, q, 2, NF))
                    nc.vector.tensor_tensor(inner_q[:, q % 2], inner[:, q % 2, :].unsqueeze(1).to_broadcast([P, Q, GROUPS]),
                                            quads[:].unsqueeze(2).to_broadcast([P, Q, GROUPS]),
                                            ALU.mult).then_inc(S["innerq_r"], 1)
                    if q >= 1:
                        rows(q - 1)
                rows(QUADS - 1)
                for n in range(TILES):
                    dve.wait_ge(S[f"res_l{n % 2}"], START + 16 * upto(r, n, 2, TILES))
                    dve.wait_ge(c_full[n % 2], START + upto(r, n, 2, TILES))
                    nc.vector.tensor_tensor(res[:, n % 2], res[:, n % 2], ps_f[n % 2][:], ALU.add
                                            ).then_inc(c_free[n % 2], 1)

        @block.scalar
        def _(act):
            with act.Fori(0, ROUNDS) as r:
                for s in range(R):
                    for k in range(C):
                        i = s * PER + k
                        act.wait_ge(m_full[i % 2], START + upto(r, i, 2, NM))
                        nc.scalar.copy(xnT[:, k, :], ps_m[i % 2][:]).then_inc(m_free[i % 2], 1)
                    for t in range(T):
                        take(act, r, (s * T + t) * C + 1)
                        take(act, r, (s * T + t) * C + 3)
                for q in range(QUADS):
                    n = 2 * q + 1
                    act.wait_ge(y_full[n % 3], START + upto(r, n, 3, NY))
                    if n >= 4:
                        act.wait_ge(y_stored[n % 4], START + 32 * before(r, n, 4, NY))
                    nc.scalar.copy(y[:, n % 4, :], ps_d[n % 3][:]).then_inc(y_free[n % 3], 1)
                for n in range(TILES):
                    act.wait_ge(c_free[n % 2], START + upto(r, n, 2, TILES))
                    act.dma_start(out_rows[r, n], res[:, n % 2]).then_inc(S[f"stored{n % 2}"], 16)


def skewed(rel, L):
    import numpy as np

    p, u = np.arange(P)[:, None], np.arange(2 * L - P)[None]
    return rel[:, p - u + 2 * L - P - 1].transpose(1, 0, 2)


def decoder_layer(nc, x, ctx_1024, attn, xattn, ffn, ident, quads, out):
    B, L, D = x.shape
    after_attn = nc.dram_tensor("after_attn", (B, L, D), F32, kind="Internal").ap()
    after_xattn = nc.dram_tensor("after_xattn", (B, L, D), F32, kind="Internal").ap()
    rows = nc.dram_tensor("expert_rows", (B // 4, 4 * L // ffn["tie"].shape[0], ffn["controller"].shape[1], D),
                          F32, kind="Internal").ap()
    nc.disable_value_cache = True
    self_attention(nc, x, after_attn, attn, ident)
    cross_attention(nc, after_attn, after_xattn, ctx_1024, xattn, ident, quads)
    expert_ffn(nc, after_xattn, out, rows, ffn, ident, quads)


def kernel(x, ctx_1024, L0_attn_Wq, L0_attn_bq, L0_attn_Wk, L0_attn_bk, L0_attn_Wv, L0_attn_bv, L0_attn_rel_emb,
           L0_xattn_fm_w, L0_xattn_fm_b, L0_xattn_fc_w, L0_xattn_fc_b, L0_ffn_controller, L0_ffn_f1, L0_ffn_bias,
           L0_ffn_f2):
    import numpy as np
    import concourse.bacc as bacc
    from concourse.bass_utils import run_bass_kernel_spmd

    nc = bacc.Bacc("TRN2", target_bir_lowering=False, num_devices=1)
    arrays = {}

    def given(name, a):
        a = np.ascontiguousarray(a)
        arrays["in_" + name] = a
        return nc.dram_tensor("in_" + name, a.shape, mybir.dt.from_np(a.dtype), kind="ExternalInput").ap()

    a = {n: np.asarray(v) for n, v in dict(
        x=x, ctx=ctx_1024, wq=L0_attn_Wq, bq=L0_attn_bq, wk=L0_attn_Wk, bk=L0_attn_bk, wv=L0_attn_Wv, bv=L0_attn_bv,
        rel=L0_attn_rel_emb, fm=L0_xattn_fm_w, fmb=L0_xattn_fm_b, fc=L0_xattn_fc_w, fcb=L0_xattn_fc_b,
        controller=L0_ffn_controller, f1=L0_ffn_f1, bias=L0_ffn_bias, f2=L0_ffn_f2).items()}
    B, L, D = a["x"].shape
    E, ES, F = a["bias"].shape
    heads, head_dim = a["rel"].shape[0], a["fm"].shape[0]
    ident = given("ident", np.eye(P, dtype=np.float32))
    quads = given("quads", np.repeat(np.eye(4, dtype=np.float32), P // 4, axis=0))
    tie = given("tie", np.linspace(0.0, 1e-6, E, dtype=np.float32))
    attn = dict(wq=given("wq", a["wq"]), wk=given("wk", a["wk"]), wv=given("wv", a["wv"]),
                bq=given("bq", a["bq"].reshape(-1, P).T), bk=given("bk", a["bk"].reshape(-1, P).T),
                bv=given("bv", a["bv"]), skewed=given("skewed", skewed(a["rel"], L)))
    xattn = dict(fm=given("fm", a["fm"].T), fb=given("fb", np.tile(a["fmb"], P // head_dim)[:, None]),
                 fb_row=given("fb_row", np.tile(a["fmb"], heads)), fc=given("fc", a["fc"].T),
                 fcb=given("fcb", a["fcb"]))
    ffn = dict(controller=given("controller", a["controller"].reshape(D, -1)), f1=given("f1", a["f1"].reshape(D, -1)),
               bias1=given("bias1", a["bias"].reshape(-1, P).T), f2=given("f2", a["f2"].reshape(-1, D)), tie=tie)
    out = nc.dram_tensor("out_0", (B, L, D), F32, kind="ExternalOutput").ap()
    decoder_layer(nc, given("x", a["x"]), given("ctx", a["ctx"]), attn, xattn, ffn, ident, quads, out)
    r = run_bass_kernel_spmd(nc, [arrays], core_ids=[0])
    return r.results[0]["out_0"]
```
